# Optimizing a Trainium2 kernel written in Bass

```python
import numpy as np
import jax
import jax.numpy as jnp

def _softmax(x, axis=-1):
    return jax.nn.softmax(x, axis=axis)

def _gelu(x):
    return jax.nn.gelu(x, approximate=True)

def _silu(x):
    return jax.nn.silu(x)

def _sigmoid(x):
    return jax.nn.sigmoid(x)

def _layernorm(x, axis=-1, eps=1e-05):
    m = jnp.mean(x, axis=axis, keepdims=True)
    v = jnp.var(x, axis=axis, keepdims=True)
    return (x - m) / jnp.sqrt(v + eps)

def _scatter_add(tgt, idx, src, axis=0):
    return tgt.at[idx].add(src)

def _segment_sum(src, seg, n):
    return jax.ops.segment_sum(src, seg, n)
kernel_name = 'mk_dlrm_tower_d1_rec_r8_26dd7d'

def setup_inputs(seed: int=0):
    np.random.seed(seed)
    _w = jnp.asarray

    def _rec_inputs():
        import jax
        import jax.numpy as jnp
        _tk = jax.random.key(seed)
        ids = jnp.stack([jax.random.randint(jax.random.fold_in(_tk, 200 + f), (512,), 0, v, jnp.int32) for f, v in enumerate([1250, 1250, 12500, 1000, 1000, 1250, 125000, 1250, 1000, 1250, 1000, 1000, 1250, 12500, 1000, 1250, 12500, 1000, 12500, 1000, 1000, 12500, 12500, 12500, 1000, 1000])], axis=1)
        tbl_0 = 0.05 * jax.random.normal(jax.random.fold_in(_tk, 500 + 0), (1250, 128), jnp.float32)
        tbl_1 = 0.05 * jax.random.normal(jax.random.fold_in(_tk, 500 + 1), (1250, 128), jnp.float32)
        tbl_2 = 0.05 * jax.random.normal(jax.random.fold_in(_tk, 500 + 2), (12500, 128), jnp.float32)
        tbl_3 = 0.05 * jax.random.normal(jax.random.fold_in(_tk, 500 + 3), (1000, 128), jnp.float32)
        tbl_4 = 0.05 * jax.random.normal(jax.random.fold_in(_tk, 500 + 4), (1000, 128), jnp.float32)
        tbl_5 = 0.05 * jax.random.normal(jax.random.fold_in(_tk, 500 + 5), (1250, 128), jnp.float32)
        tbl_6 = 0.05 * jax.random.normal(jax.random.fold_in(_tk, 500 + 6), (125000, 128), jnp.float32)
        tbl_7 = 0.05 * jax.random.normal(jax.random.fold_in(_tk, 500 + 7), (1250, 128), jnp.float32)
        tbl_8 = 0.05 * jax.random.normal(jax.random.fold_in(_tk, 500 + 8), (1000, 128), jnp.float32)
        tbl_9 = 0.05 * jax.random.normal(jax.random.fold_in(_tk, 500 + 9), (1250, 128), jnp.float32)
        tbl_10 = 0.05 * jax.random.normal(jax.random.fold_in(_tk, 500 + 10), (1000, 128), jnp.float32)
        tbl_11 = 0.05 * jax.random.normal(jax.random.fold_in(_tk, 500 + 11), (1000, 128), jnp.float32)
        tbl_12 = 0.05 * jax.random.normal(jax.random.fold_in(_tk, 500 + 12), (1250, 128), jnp.float32)
        tbl_13 = 0.05 * jax.random.normal(jax.random.fold_in(_tk, 500 + 13), (12500, 128), jnp.float32)
        tbl_14 = 0.05 * jax.random.normal(jax.random.fold_in(_tk, 500 + 14), (1000, 128), jnp.float32)
        tbl_15 = 0.05 * jax.random.normal(jax.random.fold_in(_tk, 500 + 15), (1250, 128), jnp.float32)
        tbl_16 = 0.05 * jax.random.normal(jax.random.fold_in(_tk, 500 + 16), (12500, 128), jnp.float32)
        tbl_17 = 0.05 * jax.random.normal(jax.random.fold_in(_tk, 500 + 17), (1000, 128), jnp.float32)
        tbl_18 = 0.05 * jax.random.normal(jax.random.fold_in(_tk, 500 + 18), (12500, 128), jnp.float32)
        tbl_19 = 0.05 * jax.random.normal(jax.random.fold_in(_tk, 500 + 19), (1000, 128), jnp.float32)
        tbl_20 = 0.05 * jax.random.normal(jax.random.fold_in(_tk, 500 + 20), (1000, 128), jnp.float32)
        tbl_21 = 0.05 * jax.random.normal(jax.random.fold_in(_tk, 500 + 21), (12500, 128), jnp.float32)
        tbl_22 = 0.05 * jax.random.normal(jax.random.fold_in(_tk, 500 + 22), (12500, 128), jnp.float32)
        tbl_23 = 0.05 * jax.random.normal(jax.random.fold_in(_tk, 500 + 23), (12500, 128), jnp.float32)
        tbl_24 = 0.05 * jax.random.normal(jax.random.fold_in(_tk, 500 + 24), (1000, 128), jnp.float32)
        tbl_25 = 0.05 * jax.random.normal(jax.random.fold_in(_tk, 500 + 25), (1000, 128), jnp.float32)
        _rk = jax.random.fold_in(_tk, 7)
        r_dense_features = -0.000520686 + 1.00062 * jax.random.normal(jax.random.fold_in(_rk, 101), (512, 128), jnp.float32)
        W_top1 = 0.0405887 * jax.random.normal(jax.random.fold_in(_tk, 801), (607, 512), jnp.float32)
        W_top2 = 0.0441942 * jax.random.normal(jax.random.fold_in(_tk, 802), (512, 256), jnp.float32)
        W_top3 = 0.0625 * jax.random.normal(jax.random.fold_in(_tk, 803), (256, 1), jnp.float32)
        b_top1 = jnp.zeros((512,), jnp.float32)
        b_top2 = jnp.zeros((256,), jnp.float32)
        return (r_dense_features, ids, tbl_0, tbl_1, tbl_2, tbl_3, tbl_4, tbl_5, tbl_6, tbl_7, tbl_8, tbl_9, tbl_10, tbl_11, tbl_12, tbl_13, tbl_14, tbl_15, tbl_16, tbl_17, tbl_18, tbl_19, tbl_20, tbl_21, tbl_22, tbl_23, tbl_24, tbl_25, W_top1, b_top1, W_top2, b_top2, W_top3)
    r_dense_features, ids, tbl_0, tbl_1, tbl_2, tbl_3, tbl_4, tbl_5, tbl_6, tbl_7, tbl_8, tbl_9, tbl_10, tbl_11, tbl_12, tbl_13, tbl_14, tbl_15, tbl_16, tbl_17, tbl_18, tbl_19, tbl_20, tbl_21, tbl_22, tbl_23, tbl_24, tbl_25, W_top1, b_top1, W_top2, b_top2, W_top3 = _rec_inputs()

    def _L0_rec_setup():
        import jax, jax.numpy as jnp
        import numpy as np
        F = 26
        N = F + 1
        _TRIU_I, _TRIU_J = np.triu_indices(N, k=1)
        key = jax.random.key(seed)
        k1, k2 = jax.random.split(key)
        B, D = (2048, 128)
        dense_features = jax.random.normal(k1, (B, D), dtype=jnp.float32)
        sparse_features = jax.random.normal(k2, (B, F, D), dtype=jnp.float32)
        return {'dense_features': dense_features, 'sparse_features': sparse_features}
    _L0_rec_all = _L0_rec_setup()
    _L0_rec_in = {k: v for k, v in _L0_rec_all.items() if k in ()}
    del _L0_rec_all
    return {'r_dense_features': r_dense_features, 'ids': ids, 'tbl_0': tbl_0, 'tbl_1': tbl_1, 'tbl_2': tbl_2, 'tbl_3': tbl_3, 'tbl_4': tbl_4, 'tbl_5': tbl_5, 'tbl_6': tbl_6, 'tbl_7': tbl_7, 'tbl_8': tbl_8, 'tbl_9': tbl_9, 'tbl_10': tbl_10, 'tbl_11': tbl_11, 'tbl_12': tbl_12, 'tbl_13': tbl_13, 'tbl_14': tbl_14, 'tbl_15': tbl_15, 'tbl_16': tbl_16, 'tbl_17': tbl_17, 'tbl_18': tbl_18, 'tbl_19': tbl_19, 'tbl_20': tbl_20, 'tbl_21': tbl_21, 'tbl_22': tbl_22, 'tbl_23': tbl_23, 'tbl_24': tbl_24, 'tbl_25': tbl_25, 'W_top1': W_top1, 'b_top1': b_top1, 'W_top2': W_top2, 'b_top2': b_top2, 'W_top3': W_top3}

def reference(r_dense_features, ids, tbl_0, tbl_1, tbl_2, tbl_3, tbl_4, tbl_5, tbl_6, tbl_7, tbl_8, tbl_9, tbl_10, tbl_11, tbl_12, tbl_13, tbl_14, tbl_15, tbl_16, tbl_17, tbl_18, tbl_19, tbl_20, tbl_21, tbl_22, tbl_23, tbl_24, tbl_25, W_top1, b_top1, W_top2, b_top2, W_top3):
    import jax
    import jax.numpy as jnp

    def _L0_rec_ref(dense_features, sparse_features):
        import jax, jax.numpy as jnp
        import numpy as np
        F = 26
        N = F + 1
        _TRIU_I, _TRIU_J = np.triu_indices(N, k=1)
        combined = jnp.concatenate([dense_features[:, None, :], sparse_features], axis=1)
        interactions = jnp.einsum('bnd,bmd->bnm', combined, combined)
        interactions_flat = interactions[:, _TRIU_I, _TRIU_J]
        return jnp.concatenate([dense_features, interactions_flat], axis=1)
    e = jnp.stack([tbl_0[ids[:, 0]], tbl_1[ids[:, 1]], tbl_2[ids[:, 2]], tbl_3[ids[:, 3]], tbl_4[ids[:, 4]], tbl_5[ids[:, 5]], tbl_6[ids[:, 6]], tbl_7[ids[:, 7]], tbl_8[ids[:, 8]], tbl_9[ids[:, 9]], tbl_10[ids[:, 10]], tbl_11[ids[:, 11]], tbl_12[ids[:, 12]], tbl_13[ids[:, 13]], tbl_14[ids[:, 14]], tbl_15[ids[:, 15]], tbl_16[ids[:, 16]], tbl_17[ids[:, 17]], tbl_18[ids[:, 18]], tbl_19[ids[:, 19]], tbl_20[ids[:, 20]], tbl_21[ids[:, 21]], tbl_22[ids[:, 22]], tbl_23[ids[:, 23]], tbl_24[ids[:, 24]], tbl_25[ids[:, 25]]], axis=1)
    z = _L0_rec_ref(r_dense_features, e)
    z = z.reshape(z.shape[0], -1)
    h = jnp.concatenate([z, r_dense_features], axis=1)
    h = jnp.maximum(h @ W_top1 + b_top1, 0.0)
    h = jnp.maximum(h @ W_top2 + b_top2, 0.0)
    y = h @ W_top3
    return y

_drawn_inputs = setup_inputs


def setup_inputs(seed=0):
    import zlib

    import numpy as np

    out = dict(_drawn_inputs(seed))
    spreads = {'b_top1': (0.0, 0.1), 'b_top2': (0.0, 0.1)}
    factors = {}
    for name, (base, spread) in spreads.items():
        noise = np.random.default_rng([zlib.crc32(name.encode()), seed]).standard_normal(out[name].shape)
        drawn = base * np.exp(spread * noise) if base else spread * noise
        out[name] = jnp.asarray(drawn.astype(out[name].dtype))
    for name, factor in factors.items():
        out[name] = (out[name] * factor).astype(out[name].dtype)
    return out
```

```python
from contextlib import ExitStack

import numpy as np

import concourse.bass as bass
from concourse import mybir

ALU = mybir.AluOpType
ACT = mybir.ActivationFunctionType
F32 = mybir.dt.float32
BF16 = mybir.dt.bfloat16
I32 = mybir.dt.int32
I16 = mybir.dt.int16

P = 128
B = 512
D = 128
F = 26
N = F + 1
NPAD = 32
TILES = B // P
BANK = 512
H1, H2 = 512, 256
M1, M2 = H1 // P, H2 // P

ONEHOT_TABLES = [3, 4, 10, 11, 19, 20, 24, 25]
V = 1000
CH = 8
VP = V // CH
VP_A = VP // 16 * 16
NOH = len(ONEHOT_TABLES)
RING = 3

GATHERED = [f for f in range(F) if f not in ONEHOT_TABLES]
SOURCES = [0] + [f + 1 for f in GATHERED]
GROUPS = [SOURCES[i:i + 4] for i in range(0, len(SOURCES), 4)]
GPT = len(GROUPS)
NG = GPT * TILES

TRI = 3
TRIANGLE = []
_at = 0
for _i in range(0, N, TRI):
    TRIANGLE.append((_i, N - 1 - _i, _at))
    _at += TRI * (N - 1 - _i)
ZC = -(-_at // P)
ZUSED = _at


def runs(features):
    out = []
    for slot, n in enumerate(features):
        if out and out[-1][1] + out[-1][2] == n:
            out[-1][2] += 1
        else:
            out.append([slot, n, 1])
    return out


def weight_rows():
    first_row = [D + sum(N - 1 - a for a in range(i)) for i in range(N)]
    out = []
    for i, length, at in TRIANGLE:
        for u in range(TRI):
            row, z, left = first_row[i + u], at + u * length, N - 1 - (i + u)
            if out and out[-1][0] + out[-1][2] == row and out[-1][1] + out[-1][2] == z:
                out[-1][2] += left
            elif left > 0:
                out.append([row, z, left])
    cut = []
    for row, z, left in out:
        while left:
            k = min(left, P - z % P)
            cut.append((row, z, k))
            row, z, left = row + k, z + k, left - k
    return cut


def build(nc, dense, ids, ids_by_table, tables, w1, b1, w2, b2, w3, constants, out):
    with ExitStack() as ctx:
        def sb(name, shape, dt):
            return ctx.enter_context(nc.sbuf_tensor(name, shape, dt))

        def sem(name):
            return ctx.enter_context(nc.semaphore(name))

        consts = sb("consts", [P, P + CH], F32)
        ident, row_id = consts[:, 0:P], consts[:, P:P + CH]
        ids_sb = sb("ids_sb", [P, TILES, F], I32)
        dense_sb = sb("dense_sb", [P, TILES, D], F32)
        rows_sb = sb("rows_sb", [P, TILES, len(GATHERED), D], F32)
        xt = sb("xt", [P, B, NPAD], F32)
        table_sb = sb("table_sb", [VP, RING, CH * D], F32)
        rest_sb = sb("rest_sb", [VP, RING, CH * D], F32)
        last_sb = sb("last_sb", [VP, RING, CH * D], BF16)
        idrow32 = sb("idrow32", [P, RING, B], I32)
        idrow16 = sb("idrow16", [P, RING, B], I16)
        onehot = sb("onehot", [VP, RING, CH, B], BF16)
        zz = sb("zz", [P, N + 1, NPAD], F32)
        z = sb("z", [P, ZC * P], F32)
        zt = sb("zt", [P, 2, ZC, P], F32)
        h1 = sb("h1", [P, 2, M1, P], F32)
        h2 = sb("h2", [P, 2, M2, P], F32)
        w1z = sb("w1z", [P, ZC, H1], F32)
        w1d = sb("w1d", [P, 3, H1], F32)
        w2_sb = sb("w2_sb", [P, M1, H2], F32)
        w3_sb = sb("w3_sb", [P, M2], F32)
        b1_sb = sb("b1_sb", [P, M1], F32)
        b2_sb = sb("b2_sb", [P, M2], F32)
        y_sb = sb("y_sb", [1, B], F32)

        def bank(name, banks=1):
            return ctx.enter_context(nc.psum_tensor(name, [P, banks, BANK], F32))

        ps_a = bank("ps_a", 2)
        ps_rows = bank("ps_rows", 2)
        ps_gram = bank("ps_gram", 2)
        ps_z = bank("ps_z")
        ps_h2 = bank("ps_h2")
        lookups = ps_a
        SPB = P // 4 // 2

        ids_landed = sem("ids_landed")
        consts_landed = sem("consts_landed")
        dense_landed = sem("dense_landed")
        w1d_landed = sem("w1d_landed")
        w1z_landed = sem("w1z_landed")
        layers_landed = sem("layers_landed")
        idrow_landed = [sem(f"idrow_landed{i}") for i in range(RING)]
        table_landed = [sem(f"table_landed{i}") for i in range(RING)]
        group_landed = [sem(f"group_landed{g}") for g in range(NG)]
        w1z_zeroed = sem("w1z_zeroed")
        pads_zeroed = sem("pads_zeroed")
        w1d_summed = sem("w1d_summed")
        idrow16_ready = sem("idrow16_ready")
        onehot_ready = sem("onehot_ready")
        rest_ready = sem("rest_ready")
        last_ready = sem("last_ready")
        lookup_done = sem("lookup_done")
        lookup_copied = sem("lookup_copied")
        group_turned = sem("group_turned")
        group_copied = sem("group_copied")
        gram_done = sem("gram_done")
        blocks_turned = sem("blocks_turned")
        triangle_packed = sem("triangle_packed")
        z_turned = sem("z_turned")
        z_copied = sem("z_copied")
        h1_done = sem("h1_done")
        h1_low_ready = sem("h1_low_ready")
        h1_high_ready = sem("h1_high_ready")
        h2_done = sem("h2_done")
        h2_ready = sem("h2_ready")
        y_done = sem("y_done")
        y_copied = sem("y_copied")
        stored = sem("stored")

        def diagonal(i, length):
            flat, step = zz[:, :, :].rearrange("p m n -> p (m n)"), NPAD + 1
            first = i * step + 1
            return flat[:, first:first + TRI * step].rearrange("p (r l) -> p r l", r=TRI)[:, :, 0:length]

        W1Z = weight_rows()
        block = ctx.enter_context(nc.Block())

        @block.sync
        def _(sp):
            def load_table(h):
                s, f = h % RING, ONEHOT_TABLES[h]
                if h >= RING:
                    sp.wait_ge(lookup_done, h - RING + 1)
                sp.dma_start(idrow32[:, s, :], ids_by_table[f:f + 1, :].to_broadcast([P, B])).then_inc(idrow_landed[s], 16)
                rows = tables[f].rearrange("(p c) d -> p (c d)", c=CH)
                sp.dma_start(table_sb[0:VP_A, s, :], rows[0:VP_A, :]).then_inc(table_landed[s], 16)
                sp.dma_start(table_sb[VP_A:VP, s, :], rows[VP_A:VP, :]).then_inc(table_landed[s], 16)

            sp.dma_start(ids_sb[:, :, :], ids.rearrange("(t p) f -> p t f", p=P)).then_inc(ids_landed, 16)
            sp.dma_start(consts[:, :], constants).then_inc(consts_landed, 16)
            load_table(0)
            sp.dma_start(dense_sb[:, :, :], dense.rearrange("(t p) d -> p t d", p=P)).then_inc(dense_landed, 16)
            for h in range(1, RING):
                load_table(h)
            sp.dma_start(w1d[:, 0, :], w1[0:D, :]).then_inc(w1d_landed, 16)
            sp.dma_start(w1d[:, 1, :], w1[w1.shape[0] - D:, :]).then_inc(w1d_landed, 16)
            load_table(RING)
            sp.wait_ge(w1z_zeroed, 1)
            for row, at, count in W1Z:
                sp.dma_start(w1z[at % P:at % P + count, at // P, :], w1[row:row + count, :]).then_inc(w1z_landed, 16)
            for h in range(RING + 1, NOH):
                load_table(h)
            sp.dma_start(w2_sb[:, :, :], w2.rearrange("(m p) n -> p m n", p=P)).then_inc(layers_landed, 16)
            with nc.allow_non_contiguous_dma(reason="biases and the last layer's weights: a value per partition"):
                sp.dma_start(w3_sb[:, :], w3.rearrange("(m p) o -> p (m o)", p=P)).then_inc(layers_landed, 16)
                sp.dma_start(b1_sb[:, :], b1.rearrange("(m p) -> p m", p=P)).then_inc(layers_landed, 16)
                sp.dma_start(b2_sb[:, :], b2.rearrange("(m p) -> p m", p=P)).then_inc(layers_landed, 16)
            sp.wait_ge(y_copied, TILES)
            sp.dma_start(out.rearrange("b o -> o b"), y_sb[:, :]).then_inc(stored, 16)
            sp.wait_ge(stored, 16)

        @block.gpsimd
        def _(pool):
            pool.wait_ge(ids_landed, 16)
            for t in range(TILES):
                for q, features in enumerate(GROUPS):
                    for n in features:
                        if n > 0:
                            f = n - 1
                            pool.indirect_dma_start(
                                rows_sb[:, t, GATHERED.index(f), :], None, tables[f],
                                bass.IndirectOffsetOnAxis(ids_sb[:, t, f:f + 1], 0),
                            ).then_inc(group_landed[GPT * t + q], 16)

        @block.tensor
        def _(pe):
            def lookup(h):
                s, o = h % RING, lookups[:, h % 2, :]
                if h >= 2:
                    pe.wait_ge(lookup_copied, h - 1)
                pe.wait_ge(table_landed[s], 32 * (h // RING + 1))
                high = table_sb[:, s, :].bitcast(BF16)
                middle = rest_sb[:, s, :].bitcast(BF16)
                for c in range(CH):
                    pe.wait_ge(onehot_ready, CH * h + c + 1)
                    pe.matmul(o, high[:, 2 * c * D + 1:2 * (c + 1) * D:2], onehot[:, s, c, :], start=(c == 0), stop=False)
                pe.wait_ge(rest_ready, h + 1)
                for c in range(CH):
                    pe.matmul(o, middle[:, 2 * c * D + 1:2 * (c + 1) * D:2], onehot[:, s, c, :], start=False, stop=False)
                pe.wait_ge(last_ready, h + 1)
                for c in range(CH):
                    last = pe.matmul(o, last_sb[:, s, c * D:(c + 1) * D], onehot[:, s, c, :], start=False, stop=(c == CH - 1))
                last.then_inc(lookup_done, 1)

            def turn_group(g):
                t, features = g // GPT, GROUPS[g % GPT]
                if g >= 2:
                    pe.wait_ge(group_copied, g - 1)
                if g == 0:
                    pe.wait_ge(consts_landed, 16)
                if 0 in features:
                    pe.wait_ge(dense_landed, 16)
                pe.wait_ge(group_landed[g], 16 * sum(n > 0 for n in features))
                for slot, n in enumerate(features):
                    src = rows_sb[:, t, GATHERED.index(n - 1), :] if n else dense_sb[:, t, :]
                    last = pe.transpose(ps_rows[:, g % 2, slot * P:(slot + 1) * P], src, ident)
                last.then_inc(group_turned, 1)

            def gram(t, half):
                if half == 0:
                    pe.wait_ge(group_copied, GPT * (t + 1))
                    pe.wait_ge(lookup_copied, NOH)
                    pe.wait_ge(pads_zeroed, t + 1)
                    if t:
                        pe.wait_ge(blocks_turned, t)
                for s in range(SPB):
                    for j in range(4):
                        x = xt[:, t * P + 32 * j + half * SPB + s, :]
                        last = pe.matmul(ps_gram[32 * j:32 * j + 32, half, s * N:(s + 1) * N], x, x[:, 0:N],
                                         start=True, stop=True)
                if half:
                    last.then_inc(gram_done, 1)

            def turn_z(t):
                pe.wait_ge(triangle_packed, 2 * (t + 1))
                if t:
                    pe.wait_ge(z_copied, t)
                for c in range(ZC):
                    last = pe.transpose(ps_z[:, 0, c * P:(c + 1) * P], z[:, c * P:(c + 1) * P], ident)
                last.then_inc(z_turned, 1)

            def layer1_dense(t):
                if t == 0:
                    pe.wait_ge(w1d_summed, 1)
                else:
                    pe.wait_ge(h1_low_ready, t)
                    pe.wait_ge(h1_high_ready, t)
                for m in range(M1):
                    pe.matmul(ps_a[:, m // 2, (m % 2) * P:(m % 2 + 1) * P], w1d[:, 2, m * P:(m + 1) * P],
                              xt[:, t * P:(t + 1) * P, 0], start=(m % 2 == 0), stop=False, skip_group_check=True)

            def layer1_pairs(t):
                if t == 0:
                    pe.wait_ge(w1z_landed, 16 * len(W1Z))
                pe.wait_ge(z_copied, t + 1)
                for m in range(M1):
                    for c in range(ZC):
                        last = pe.matmul(ps_a[:, m // 2, (m % 2) * P:(m % 2 + 1) * P], w1z[:, c, m * P:(m + 1) * P],
                                         zt[:, t % 2, c, :], start=False, stop=(c == ZC - 1), skip_group_check=True)
                    if m % 2:
                        last.then_inc(h1_done, 1)

            def layer2(t):
                pe.wait_ge(layers_landed, 64)
                if t:
                    pe.wait_ge(y_copied, t)
                for k in range(M1):
                    if k == 0:
                        pe.wait_ge(h1_low_ready, t + 1)
                    if k == M1 // 2:
                        pe.wait_ge(h1_high_ready, t + 1)
                    for m in range(M2):
                        last = pe.matmul(ps_h2[:, 0, m * P:(m + 1) * P], w2_sb[:, k, m * P:(m + 1) * P], h1[:, t % 2, k, :],
                                         start=(k == 0 and m == 0), stop=(k == M1 - 1), skip_group_check=True)
                last.then_inc(h2_done, 1)

            def layer3(t):
                pe.wait_ge(h2_ready, t + 1)
                for k in range(M2):
                    last = pe.matmul(ps_h2[0:1, 0, H2:H2 + P], w3_sb[:, k:k + 1], h2[:, t % 2, k, :],
                                     start=(k == 0), stop=(k == M2 - 1))
                last.then_inc(y_done, 1)

            for h in range(NOH):
                lookup(h)
                turn_group(h)
            for g in range(NOH, 2 * GPT):
                turn_group(g)
            gram(0, 0)
            gram(0, 1)
            for t in range(TILES):
                if t + 1 < TILES:
                    if t == 0:
                        layer1_dense(t)
                    turn_z(t)
                    if t:
                        layer1_dense(t)
                    gram(t + 1, 0)
                    layer1_pairs(t)
                    gram(t + 1, 1)
                    layer2(t)
                    if t + 2 < TILES:
                        for g in range(GPT * (t + 2), GPT * (t + 3)):
                            turn_group(g)
                    layer3(t)
                else:
                    layer1_dense(t)
                    turn_z(t)
                    layer1_pairs(t)
                    layer2(t)
                    layer3(t)

        COPIES_ON_SCALAR = 4

        @block.vector
        def _(dve):
            def zero_pads(t):
                dve.memset(xt[:, t * P:(t + 1) * P, N:NPAD], 0.0).then_inc(pads_zeroed, 1)

            dve.memset(w1z[:, :, :], 0.0).then_inc(w1z_zeroed, 1)
            zero_pads(0)
            dve.wait_ge(consts_landed, 16)
            for h in range(NOH):
                s = h % RING
                dve.wait_ge(idrow16_ready, h + 1)
                if h >= RING:
                    dve.wait_ge(lookup_done, h - RING + 1)
                for c in range(CH):
                    dve.tensor_scalar(onehot[:, s, c, :], idrow16[0:VP, s, :], row_id[0:VP, c:c + 1], None,
                                      ALU.is_equal).then_inc(onehot_ready, 1)
                dve.wait_ge(table_landed[s], 32 * (h // RING + 1))
                dve.tensor_tensor(rest_sb[:, s, :], table_sb[:, s, :], table_sb[:, s, :].bitcast(BF16)[:, 1:2 * CH * D:2],
                                  ALU.subtract).then_inc(rest_ready, 1)
                dve.wait_ge(rest_ready, h + 1)
                dve.tensor_tensor(last_sb[:, s, :], rest_sb[:, s, :], rest_sb[:, s, :].bitcast(BF16)[:, 1:2 * CH * D:2],
                                  ALU.subtract).then_inc(last_ready, 1)
            dve.memset(z[:, ZUSED:], 0.0)
            dve.wait_ge(w1d_landed, 32)
            dve.tensor_tensor(w1d[:, 2, :], w1d[:, 0, :], w1d[:, 1, :], ALU.add).then_inc(w1d_summed, 1)
            for t in range(1, TILES):
                zero_pads(t)

            for t in range(TILES):
                dve.wait_ge(gram_done, t + 1)
                if t:
                    dve.wait_ge(triangle_packed, 2 * t)
                dve.transpose(zz[:, 0:N, :], ps_gram[:, :, 0:SPB * N].rearrange("p k (s m) -> p m k s", m=N)) \
                   .then_inc(blocks_turned, 1)
                dve.wait_ge(blocks_turned, t + 1)
                if t:
                    dve.wait_ge(z_turned, t)
                for i, length, at in TRIANGLE[:len(TRIANGLE) - COPIES_ON_SCALAR]:
                    last = dve.tensor_copy(
                        z[:, at:at + TRI * length].rearrange("p (r l) -> p r l", r=TRI),
                        diagonal(i, length))
                last.then_inc(triangle_packed, 1)
                dve.wait_ge(h1_done, 2 * (t + 1))
                if t == 0:
                    dve.wait_ge(layers_landed, 64)
                if t >= 2:
                    dve.wait_ge(h2_done, t - 1)
                for m in range(M1 // 2, M1):
                    last = dve.tensor_scalar(h1[:, t % 2, m, :], ps_a[:, 1, (m % 2) * P:(m % 2 + 1) * P],
                                             b1_sb[:, m:m + 1], 0.0, ALU.add, ALU.max)
                last.then_inc(h1_high_ready, 1)

        @block.scalar
        def _(act):
            def narrow_ids(h):
                s = h % RING
                act.wait_ge(idrow_landed[s], 16 * (h // RING + 1))
                if h >= RING:
                    act.wait_ge(onehot_ready, CH * (h - RING + 1))
                act.copy(idrow16[:, s, :], idrow32[:, s, :]).then_inc(idrow16_ready, 1)

            def copy_lookup(h):
                act.wait_ge(lookup_done, h + 1)
                act.copy(xt[:, :, ONEHOT_TABLES[h] + 1], lookups[:, h % 2, :]).then_inc(lookup_copied, 1)

            def copy_group(g):
                t = g // GPT
                act.wait_ge(group_turned, g + 1)
                for slot, n, count in runs(GROUPS[g % GPT]):
                    last = act.copy(
                        xt[:, t * P:(t + 1) * P, n:n + count],
                        ps_rows[:, g % 2, slot * P:(slot + count) * P].rearrange("p (n b) -> p b n", n=count))
                last.then_inc(group_copied, 1)

            def pack_triangle(t):
                act.wait_ge(blocks_turned, t + 1)
                if t:
                    act.wait_ge(z_turned, t)
                for i, length, at in TRIANGLE[len(TRIANGLE) - COPIES_ON_SCALAR:]:
                    last = act.copy(z[:, at:at + TRI * length].rearrange("p (r l) -> p r l", r=TRI),
                                    diagonal(i, length))
                last.then_inc(triangle_packed, 1)

            def copy_z(t):
                act.wait_ge(z_turned, t + 1)
                if t >= 2:
                    act.wait_ge(h1_done, 2 * (t - 1))
                act.copy(zt[:, t % 2, :, :], ps_z[:, 0, 0:ZC * P].rearrange("p (c b) -> p c b", c=ZC)).then_inc(z_copied, 1)

            def relu1_low(t):
                act.wait_ge(h1_done, 2 * t + 1)
                if t == 0:
                    act.wait_ge(layers_landed, 64)
                if t >= 2:
                    act.wait_ge(h2_done, t - 1)
                for m in range(M1 // 2):
                    last = act.activation(h1[:, t % 2, m, :], ps_a[:, 0, m * P:(m + 1) * P], ACT.Relu, bias=b1_sb[:, m:m + 1])
                last.then_inc(h1_low_ready, 1)

            def relu2(t):
                act.wait_ge(h2_done, t + 1)
                if t >= 2:
                    act.wait_ge(y_done, t - 1)
                for m in range(M2):
                    last = act.activation(h2[:, t % 2, m, :], ps_h2[:, 0, m * P:(m + 1) * P], ACT.Relu, bias=b2_sb[:, m:m + 1])
                last.then_inc(h2_ready, 1)

            def copy_y(t):
                act.wait_ge(y_done, t + 1)
                act.copy(y_sb[:, t * P:(t + 1) * P], ps_h2[0:1, 0, H2:H2 + P]).then_inc(y_copied, 1)

            narrow_ids(0)
            narrow_ids(1)
            for h in range(NOH):
                if h + 2 < NOH:
                    narrow_ids(h + 2)
                copy_lookup(h)
                copy_group(h)
            for g in range(NOH, 2 * GPT):
                copy_group(g)
            for t in range(TILES):
                pack_triangle(t)
                copy_z(t)
                relu1_low(t)
                if t + 2 < TILES:
                    for g in range(GPT * (t + 2), GPT * (t + 3)):
                        copy_group(g)
                relu2(t)
                copy_y(t)


_INPUTS = ["r_dense_features", "ids"] + [f"tbl_{f}" for f in range(F)] + ["W_top1", "b_top1", "W_top2", "b_top2", "W_top3"]


def kernel(**inputs):
    import concourse.bacc as bacc
    from concourse.bass_utils import run_bass_kernel_spmd

    nc = bacc.Bacc("TRN2", target_bir_lowering=False, num_devices=1)
    arrays = {name: np.ascontiguousarray(inputs[name]) for name in _INPUTS}
    arrays["ids_by_table"] = np.ascontiguousarray(np.asarray(inputs["ids"]).T)
    constants = np.zeros((P, P + CH), np.float32)
    constants[:, 0:P] = np.eye(P, dtype=np.float32)
    constants[:, P:] = np.arange(P * CH, dtype=np.float32).reshape(P, CH)
    arrays["constants"] = constants
    a = {name: nc.dram_tensor(name, x.shape, mybir.dt.from_np(x.dtype), kind="ExternalInput").ap()
         for name, x in arrays.items()}
    out = nc.dram_tensor("y", (B, 1), F32, kind="ExternalOutput").ap()
    build(nc, a["r_dense_features"], a["ids"], a["ids_by_table"], [a[f"tbl_{f}"] for f in range(F)],
          a["W_top1"], a["b_top1"], a["W_top2"], a["b_top2"], a["W_top3"], a["constants"], out)
    result = run_bass_kernel_spmd(nc, [arrays], core_ids=[0])
    return result.results[0]["y"]
```

```python
from contextlib import ExitStack

import numpy as np

import concourse.bass as bass
from concourse import mybir

ALU = mybir.AluOpType
ACT = mybir.ActivationFunctionType
F32 = mybir.dt.float32
F32R = mybir.dt.float32r
BF16 = mybir.dt.bfloat16
I32 = mybir.dt.int32

P = 128
B = 512
D = 128
F = 26
N = F + 1
NPAD = 32
TILES = B // P
BANK = 512
H1, H2 = 512, 256
M1, M2 = H1 // P, H2 // P

ONEHOT_TABLES = [4, 10, 11, 19, 20, 24, 25, 3, 8, 14]
LOOKUP_FROM = [0] * 8 + [P, 2 * P]
V = 1000
CH = 8
CH_V = CH - 1
VP = V // CH
VP_A = VP // 16 * 16
NOH = len(ONEHOT_TABLES)
WHOLE = LOOKUP_FROM.count(0)
TABLE_RING = 4
WORK_RING = 2
ROWS_RING = 3

def is_gathered(f, t):
    return f not in ONEHOT_TABLES or t * P < LOOKUP_FROM[ONEHOT_TABLES.index(f)]


GATHERED = [f for f in range(F) if is_gathered(f, 0)]
SOURCES = [[f + 1 for f in GATHERED if is_gathered(f, t)] for t in range(TILES)]
GROUPS = [(t, s[i:i + 4]) for t, s in enumerate(SOURCES) for i in range(0, len(s), 4)]
GROUPS[-1:] = [(TILES - 1, GROUPS[-1][1][:-1]), (TILES - 1, GROUPS[-1][1][-1:])]

AFTER_LOOKUP = [[], [0], [1], [2], [3], [4], [5], [6, 7], [8], [9, 10]]
AT_START = [[], [], [17, 18]]
IN_MIDDLE = [[11], [14], []]
AT_END = [[12, 13], [15], []]
AFTER_Z = [[], [16], []]
ORDER = sum(AFTER_LOOKUP, [])
for _t in range(TILES - 1):
    ORDER += AT_START[_t] + IN_MIDDLE[_t] + AT_END[_t] + AFTER_Z[_t]
assert ORDER == list(range(len(GROUPS)))
GROUPS_UP_TO = [sum(t <= tile for t, _ in GROUPS) for tile in range(TILES)]

WARM_UP = 14

HIGH, LOW = PARTS = range(2)

TRI = 3
TRIANGLE = []
_at = 0
for _i in range(0, N, TRI):
    TRIANGLE.append((_i, N - 1 - _i, _at))
    _at += TRI * (N - 1 - _i)
ZC = -(-_at // P)
ZUSED = _at


def runs(features):
    out = []
    for slot, n in enumerate(features):
        if out and out[-1][1] + out[-1][2] == n:
            out[-1][2] += 1
        else:
            out.append([slot, n, 1])
    return out


def weight_rows():
    first_row = [D + sum(N - 1 - a for a in range(i)) for i in range(N)]
    out = []
    for i, length, at in TRIANGLE:
        for u in range(TRI):
            row, z, left = first_row[i + u], at + u * length, N - 1 - (i + u)
            if out and out[-1][0] + out[-1][2] == row and out[-1][1] + out[-1][2] == z:
                out[-1][2] += left
            elif left > 0:
                out.append([row, z, left])
    cut = []
    for row, z, left in out:
        while left:
            k = min(left, P - z % P)
            cut.append((row, z, k))
            row, z, left = row + k, z + k, left - k
    return cut


def build(nc, dense_by_column, ids, ids_by_table, tables, w1, b1, w2, b2, w3, identity, table_rows, out):
    with ExitStack() as ctx:
        def sb(name, shape, dt):
            return ctx.enter_context(nc.sbuf_tensor(name, shape, dt))

        def sem(name):
            return ctx.enter_context(nc.semaphore(name))

        ident_sb = sb("ident_sb", [P, P], F32)
        row_id = sb("row_id", [P, CH], F32)
        minus_row_id = sb("minus_row_id", [P, 1], F32)
        distance = sb("distance", [VP, B], F32)
        ident = ident_sb[:, :]
        nothing = sb("nothing", [P, BANK], BF16)
        ids_sb = sb("ids_sb", [P, TILES, F], I32)
        dense_sb = sb("dense_sb", [D, B], F32)
        rows_sb = sb("rows_sb", [P, ROWS_RING, len(GATHERED), D], F32)
        xt = sb("xt", [P, B, N], F32)
        table_sb = sb("table_sb", [VP, TABLE_RING, CH * D], F32)
        parts_sb = [sb(f"part{i}_sb", [VP, WORK_RING, CH * D], F32R) for i in PARTS]
        idrow = sb("idrow", [P, TABLE_RING, B], I32)
        onehot = sb("onehot", [VP, WORK_RING, CH, B], F32R)
        zz = sb("zz", [P, N + 1, NPAD], F32)
        z = sb("z", [P, ZC * P], F32)
        zt = sb("zt", [P, 2, ZC, P], F32)
        h1 = sb("h1", [P, 2, M1, P], F32)
        h2 = sb("h2", [P, 2, M2, P], F32)
        w1z = sb("w1z", [P, ZC, H1], F32)
        w1d = sb("w1d", [P, 3, H1], F32)
        w2_sb = sb("w2_sb", [P, M1, H2], F32)
        w3_sb = sb("w3_sb", [P, M2], F32)
        b1_sb = sb("b1_sb", [P, M1], F32)
        b2_sb = sb("b2_sb", [P, M2], F32)
        y_sb = sb("y_sb", [1, B], F32)

        def bank(name, banks=1):
            return ctx.enter_context(nc.psum_tensor(name, [P, banks, BANK], F32))

        ps_a = bank("ps_a", 2)
        ps_rows = bank("ps_rows", 2)
        ps_gram = bank("ps_gram", 2)
        ps_z = bank("ps_z")
        ps_h2 = bank("ps_h2")
        SPB = P // 4 // 2

        ids_landed = sem("ids_landed")
        ident_landed = sem("ident_landed")
        row_id_landed = sem("row_id_landed")
        dense_landed = sem("dense_landed")
        w1d_landed = sem("w1d_landed")
        w1z_landed = sem("w1z_landed")
        layers_landed = sem("layers_landed")
        idrow_landed = [sem(f"idrow_landed{i}") for i in range(TABLE_RING)]
        table_landed = [sem(f"table_landed{i}") for i in range(TABLE_RING)]
        group_landed = [sem(f"group_landed{g}") for g in range(len(GROUPS))]
        nothing_zeroed = sem("nothing_zeroed")
        w1z_zeroed = sem("w1z_zeroed")
        gram_zeroed = sem("gram_zeroed")
        w1d_summed = sem("w1d_summed")
        onehot_ready = sem("onehot_ready")
        last_onehot_ready = sem("last_onehot_ready")
        dense_copied = sem("dense_copied")
        row_id_negated = sem("row_id_negated")
        distance_ready = sem("distance_ready")
        part_ready = [sem(f"part{i}_ready") for i in PARTS]
        lookup_done = sem("lookup_done")
        lookup_copied = sem("lookup_copied")
        group_turned = sem("group_turned")
        group_copied = sem("group_copied")
        gram_done = sem("gram_done")
        blocks_turned = sem("blocks_turned")
        first_chunk_packed = sem("first_chunk_packed")
        triangle_packed = sem("triangle_packed")
        z_turned = sem("z_turned")
        z_copied = sem("z_copied")
        h1_done = sem("h1_done")
        h1_low_ready = sem("h1_low_ready")
        h1_high_ready = sem("h1_high_ready")
        h2_done = sem("h2_done")
        h2_ready = sem("h2_ready")
        y_done = sem("y_done")
        y_copied = sem("y_copied")
        stored = sem("stored")

        def diagonal(i, length):
            flat, step = zz[:, :, :].rearrange("p m n -> p (m n)"), NPAD + 1
            first = i * step + 1
            return flat[:, first:first + TRI * step].rearrange("p (r l) -> p r l", r=TRI)[:, :, 0:length]

        def z_bank(t, c):
            return ps_rows[:, 0, :] if t == TILES - 1 and c == 0 else ps_z[:, 0, :]

        def h2_block(t, m):
            return ps_rows[:, 1, 0:P] if t == TILES - 1 and m == M2 - 1 else ps_h2[:, 0, m * P:(m + 1) * P]

        W1Z = weight_rows()
        block = ctx.enter_context(nc.Block())

        @block.sync
        def _(sp):
            def load_table(h):
                s, f = h % TABLE_RING, ONEHOT_TABLES[h]
                if h >= TABLE_RING:
                    sp.wait_ge(lookup_done, h - TABLE_RING + 1)
                sp.dma_start(idrow[:, s, :], ids_by_table[f:f + 1, :].to_broadcast([P, B])).then_inc(idrow_landed[s], 16)
                rows = tables[f].rearrange("(p c) d -> p (c d)", c=CH)
                sp.dma_start(table_sb[0:VP_A, s, :], rows[0:VP_A, :]).then_inc(table_landed[s], 16)
                sp.dma_start(table_sb[VP_A:VP, s, :], rows[VP_A:VP, :]).then_inc(table_landed[s], 16)

            sp.dma_start(ids_sb[:, :, :], ids.rearrange("(t p) f -> p t f", p=P)).then_inc(ids_landed, 16)
            sp.dma_start(row_id[:, :], table_rows).then_inc(row_id_landed, 16)
            load_table(0)
            sp.dma_start(ident_sb[:, :], identity).then_inc(ident_landed, 16)
            sp.dma_start(dense_sb[:, :], dense_by_column).then_inc(dense_landed, 16)
            for h in range(1, TABLE_RING):
                load_table(h)
            sp.wait_ge(w1z_zeroed, 1)
            per_table = -(-len(W1Z) // (NOH - TABLE_RING))
            for h in range(TABLE_RING, NOH):
                load_table(h)
                if h == TABLE_RING:
                    sp.dma_start(w1d[:, 0, :], w1[0:D, :]).then_inc(w1d_landed, 16)
                    sp.dma_start(w1d[:, 1, :], w1[w1.shape[0] - D:, :]).then_inc(w1d_landed, 16)
                first = (h - TABLE_RING) * per_table
                for row, at, count in W1Z[first:first + per_table]:
                    sp.dma_start(w1z[at % P:at % P + count, at // P, :], w1[row:row + count, :]).then_inc(w1z_landed, 16)
            sp.dma_start(w2_sb[:, :, :], w2.rearrange("(m p) n -> p m n", p=P)).then_inc(layers_landed, 16)
            with nc.allow_non_contiguous_dma(reason="biases and the last layer's weights: a value per partition"):
                sp.dma_start(w3_sb[:, :], w3.rearrange("(m p) o -> p (m o)", p=P)).then_inc(layers_landed, 16)
                sp.dma_start(b1_sb[:, :], b1.rearrange("(m p) -> p m", p=P)).then_inc(layers_landed, 16)
                sp.dma_start(b2_sb[:, :], b2.rearrange("(m p) -> p m", p=P)).then_inc(layers_landed, 16)
            sp.wait_ge(y_copied, TILES)
            sp.dma_start(out.rearrange("b o -> o b"), y_sb[:, :]).then_inc(stored, 16)
            sp.wait_ge(stored, 16)

        @block.gpsimd
        def _(pool):
            pool.wait_ge(ids_landed, 16)
            for g, (t, features) in enumerate(GROUPS):
                if t >= ROWS_RING and t != GROUPS[g - 1][0]:
                    pool.wait_ge(group_turned, GROUPS_UP_TO[t - ROWS_RING])
                for n in features:
                    f = n - 1
                    pool.indirect_dma_start(
                        rows_sb[:, t % ROWS_RING, GATHERED.index(f), :], None, tables[f],
                        bass.IndirectOffsetOnAxis(ids_sb[:, t, f:f + 1], 0),
                    ).then_inc(group_landed[g], 16)

        @block.tensor
        def _(pe):
            def lookup(h, parts=PARTS):
                w, lo = h % WORK_RING, LOOKUP_FROM[h]
                if HIGH in parts and h >= 2:
                    pe.wait_ge(lookup_copied, h - 1)
                for part in parts:
                    pe.wait_ge(part_ready[part], h + 1)
                    for c in range(CH):
                        if part == HIGH and c < CH_V:
                            pe.wait_ge(onehot_ready, CH_V * h + c + 1)
                        elif part == HIGH:
                            pe.wait_ge(last_onehot_ready, h + 1)
                        last = pe.matmul(ps_a[:, h % 2, lo:], parts_sb[part][:, w, c * D:(c + 1) * D],
                                         onehot[:, w, c, lo:], start=(part == HIGH and c == 0),
                                         stop=(part == LOW and c == CH - 1))
                if LOW in parts:
                    last.then_inc(lookup_done, 1)

            def turn_group(g):
                t, features = GROUPS[g]
                if g >= 2:
                    pe.wait_ge(group_copied, g - 1)
                if g == 0:
                    pe.wait_ge(ident_landed, 16)
                pe.wait_ge(group_landed[g], 16 * len(features))
                for slot, n in enumerate(features):
                    last = pe.transpose(ps_rows[:, g % 2, slot * P:(slot + 1) * P],
                                        rows_sb[:, t % ROWS_RING, GATHERED.index(n - 1), :], ident)
                last.then_inc(group_turned, 1)

            def gram(t, quarter):
                if quarter == 0:
                    pe.wait_ge(group_copied, GROUPS_UP_TO[t])
                    if t == 0:
                        pe.wait_ge(dense_copied, 1)
                    pe.wait_ge(lookup_copied, sum(lo < (t + 1) * P for lo in LOOKUP_FROM))
                    if t == 0:
                        pe.wait_ge(gram_zeroed, 1)
                    if t:
                        pe.wait_ge(blocks_turned, t)
                for b in range(quarter * 8, quarter * 8 + 8):
                    k, s = b // SPB, b % SPB
                    for j in range(4):
                        x = xt[:, t * P + 32 * j + b, :]
                        last = pe.matmul(ps_gram[NPAD * j:NPAD * j + N, k, s * N:(s + 1) * N], x, x, start=True, stop=True)
                if quarter == 3:
                    last.then_inc(gram_done, 1)

            def turn_z(t, chunks):
                if t < TILES - 1:
                    pe.wait_ge(triangle_packed, t + 1)
                elif 0 in chunks:
                    pe.wait_ge(first_chunk_packed, 1)
                else:
                    pe.wait_ge(triangle_packed, t + 2)
                if t:
                    pe.wait_ge(z_copied, t)
                for c in chunks:
                    last = pe.transpose(z_bank(t, c)[:, c * P:(c + 1) * P], z[:, c * P:(c + 1) * P], ident)
                last.then_inc(z_turned, 1)

            def layer1_dense(t):
                if t == 0:
                    pe.wait_ge(w1d_summed, 1)
                    pe.wait_ge(lookup_copied, NOH)
                else:
                    pe.wait_ge(h1_low_ready, t)
                    pe.wait_ge(h1_high_ready, t)
                for m in range(M1):
                    pe.matmul(ps_a[:, m // 2, (m % 2) * P:(m % 2 + 1) * P], w1d[:, 2, m * P:(m + 1) * P],
                              dense_sb[:, t * P:(t + 1) * P], start=(m % 2 == 0), stop=False, skip_group_check=True)

            def layer1_pairs(t, k, chunks=range(ZC)):
                if k == 0:
                    if t == 0:
                        pe.wait_ge(w1z_landed, 16 * len(W1Z))
                    pe.wait_ge(z_copied, t + 1 + (t == TILES - 1 and ZC - 1 in chunks))
                for m in range(2 * k, 2 * k + 2):
                    for c in chunks:
                        last = pe.matmul(ps_a[:, k, (m % 2) * P:(m % 2 + 1) * P], w1z[:, c, m * P:(m + 1) * P],
                                         zt[:, t % 2, c, :], start=False, stop=(c == ZC - 1), skip_group_check=True)
                if ZC - 1 in chunks:
                    last.then_inc(h1_done, 1)

            def layer2(t, half):
                if half == 0:
                    pe.wait_ge(layers_landed, 64)
                    if t:
                        pe.wait_ge(y_copied, t)
                pe.wait_ge(h1_high_ready if half else h1_low_ready, t + 1)
                for k in range(half * M1 // 2, (half + 1) * M1 // 2):
                    for m in range(M2):
                        last = pe.matmul(ps_h2[:, 0, m * P:(m + 1) * P], w2_sb[:, k, m * P:(m + 1) * P], h1[:, t % 2, k, :],
                                         start=(k == 0 and m == 0), stop=(k == M1 - 1), skip_group_check=True)
                if half:
                    last.then_inc(h2_done, 1)

            def layer2_last():
                t = TILES - 1
                pe.wait_ge(y_copied, t)
                for half, ready in enumerate((h1_low_ready, h1_high_ready)):
                    pe.wait_ge(ready, t + 1)
                    for m in range(M2):
                        for k in range(half * M1 // 2, (half + 1) * M1 // 2):
                            last = pe.matmul(h2_block(t, m), w2_sb[:, k, m * P:(m + 1) * P], h1[:, t % 2, k, :],
                                             start=(k == 0), stop=(k == M1 - 1))
                        if half:
                            last.then_inc(h2_done, 1)

            def layer3(t):
                for k in range(M2):
                    if t == TILES - 1:
                        pe.wait_ge(h2_ready, M2 * t + k + 1)
                    elif k == 0:
                        pe.wait_ge(h2_ready, M2 * (t + 1))
                    last = pe.matmul(ps_h2[0:1, 0, H2:H2 + P], w3_sb[:, k:k + 1], h2[:, t % 2, k, :],
                                     start=(k == 0), stop=(k == M2 - 1))
                last.then_inc(y_done, 1)

            pe.wait_ge(nothing_zeroed, 1)
            for _ in range(WARM_UP):
                pe.matmul(ps_z[:, 0, :], nothing[:, 0:P], nothing[:, :], start=True, stop=True)

            for h in range(WHOLE):
                lookup(h)
                for g in AFTER_LOOKUP[h]:
                    turn_group(g)
            for quarter in range(4):
                gram(0, quarter)
            for h in range(WHOLE, NOH):
                lookup(h)
                for g in AFTER_LOOKUP[h]:
                    turn_group(g)
            turn_z(0, range(ZC))
            layer1_dense(0)
            for t in range(TILES - 1):
                if t < TILES - 2:
                    for g in AT_START[t]:
                        turn_group(g)
                    gram(t + 1, 0)
                    gram(t + 1, 1)
                    layer1_pairs(t, 0)
                    for g in IN_MIDDLE[t]:
                        turn_group(g)
                    layer1_pairs(t, 1)
                    gram(t + 1, 2)
                    gram(t + 1, 3)
                    layer2(t, 0)
                    layer2(t, 1)
                    for g in AT_END[t]:
                        turn_group(g)
                    layer1_dense(t + 1)
                    turn_z(t + 1, range(ZC))
                    for g in AFTER_Z[t]:
                        turn_group(g)
                    layer3(t)
                else:
                    layer1_pairs(t, 0)
                    layer1_pairs(t, 1)
                    for g in AT_START[t]:
                        turn_group(g)
                    layer2(t, 0)
                    for quarter in range(4):
                        gram(t + 1, quarter)
                    layer2(t, 1)
                    layer1_dense(t + 1)
                    turn_z(t + 1, range(1))
                    turn_z(t + 1, range(1, ZC))
            t = TILES - 1
            for chunks in (range(1), range(1, ZC)):
                layer1_pairs(t, 0, chunks)
                layer1_pairs(t, 1, chunks)
                if 0 in chunks:
                    layer3(t - 1)
            layer2_last()
            layer3(t)

        BY_VECTOR = [len(TRIANGLE)] * (TILES - 1) + [len(TRIANGLE) - 4]

        @block.vector
        def _(dve):
            dve.memset(nothing[:, :], 0.0).then_inc(nothing_zeroed, 1)
            dve.memset(w1z[:, :, :], 0.0).then_inc(w1z_zeroed, 1)
            dve.memset(ps_gram[:, :, 0:SPB * N], 0.0).then_inc(gram_zeroed, 1)
            dve.wait_ge(row_id_landed, 16)

            def prepare_lookup(h):
                s, w = h % TABLE_RING, h % WORK_RING
                dve.wait_ge(idrow_landed[s], 16 * (h // TABLE_RING + 1))
                if h >= WORK_RING:
                    dve.wait_ge(lookup_done, h - WORK_RING + 1)
                for c in range(CH_V):
                    dve.tensor_scalar(onehot[:, w, c, LOOKUP_FROM[h]:], idrow[0:VP, s, LOOKUP_FROM[h]:],
                                      row_id[0:VP, c:c + 1], None, ALU.is_equal).then_inc(onehot_ready, 1)
                dve.wait_ge(part_ready[HIGH], h + 1)
                dve.tensor_tensor(parts_sb[LOW][:, w, :], table_sb[:, s, :], parts_sb[HIGH][:, w, :].bitcast(F32),
                                  ALU.subtract).then_inc(part_ready[LOW], 1)
            for h in range(NOH):
                prepare_lookup(h)
            dve.memset(z[:, ZUSED:], 0.0)
            dve.wait_ge(w1d_landed, 32)
            dve.tensor_tensor(w1d[:, 2, :], w1d[:, 0, :], w1d[:, 1, :], ALU.add).then_inc(w1d_summed, 1)

            for t in range(TILES):
                dve.wait_ge(gram_done, t + 1)
                if t:
                    dve.wait_ge(triangle_packed, t)
                dve.transpose(zz[:, 0:N, :], ps_gram[:, :, 0:SPB * N].rearrange("p k (s m) -> p m k s", m=N)) \
                   .then_inc(blocks_turned, 1)
                dve.wait_ge(blocks_turned, t + 1)
                if t:
                    dve.wait_ge(z_turned, t)
                for i, length, at in TRIANGLE[:BY_VECTOR[t]]:
                    last = dve.tensor_copy(
                        z[:, at:at + TRI * length].rearrange("p (r l) -> p r l", r=TRI),
                        diagonal(i, length))
                    if t == TILES - 1 and at < P <= at + TRI * length:
                        last.then_inc(first_chunk_packed, 1)
                last.then_inc(triangle_packed, 1)
                dve.wait_ge(h1_done, 2 * (t + 1))
                if t == 0:
                    dve.wait_ge(layers_landed, 64)
                if t >= 2:
                    dve.wait_ge(h2_done, t - 1)
                for m in range(M1 // 2, M1):
                    last = dve.tensor_scalar(h1[:, t % 2, m, :], ps_a[:, 1, (m % 2) * P:(m % 2 + 1) * P],
                                             b1_sb[:, m:m + 1], 0.0, ALU.add, ALU.max)
                last.then_inc(h1_high_ready, 1)

        @block.scalar
        def _(act):
            def round_table(h):
                s, w = h % TABLE_RING, h % WORK_RING
                act.wait_ge(table_landed[s], 32 * (h // TABLE_RING + 1))
                if h >= WORK_RING:
                    act.wait_ge(lookup_done, h - WORK_RING + 1)
                act.copy(parts_sb[HIGH][:, w, :], table_sb[:, s, :]).then_inc(part_ready[HIGH], 1)

            def last_onehot(h):
                s, w, lo = h % TABLE_RING, h % WORK_RING, LOOKUP_FROM[h]
                act.wait_ge(idrow_landed[s], 16 * (h // TABLE_RING + 1))
                if h == 0:
                    act.wait_ge(row_id_negated, 1)
                else:
                    act.wait_ge(last_onehot_ready, h)
                act.activation(distance[:, lo:], idrow[0:VP, s, lo:], ACT.Abs, bias=minus_row_id[0:VP, :]) \
                   .then_inc(distance_ready, 1)
                if h >= WORK_RING:
                    act.wait_ge(lookup_done, h - WORK_RING + 1)
                act.wait_ge(distance_ready, h + 1)
                act.activation(onehot[:, w, CH - 1, lo:], distance[:, lo:], ACT.Relu, bias=1.0, scale=-1.0) \
                   .then_inc(last_onehot_ready, 1)

            def copy_lookup(h):
                act.wait_ge(lookup_done, h + 1)
                lo = LOOKUP_FROM[h]
                act.copy(xt[:, lo:, ONEHOT_TABLES[h] + 1], ps_a[:, h % 2, lo:]).then_inc(lookup_copied, 1)

            def copy_group(g):
                t, features = GROUPS[g]
                act.wait_ge(group_turned, g + 1)
                for slot, n, count in runs(features):
                    last = act.copy(
                        xt[:, t * P:(t + 1) * P, n:n + count],
                        ps_rows[:, g % 2, slot * P:(slot + count) * P].rearrange("p (n b) -> p b n", n=count))
                last.then_inc(group_copied, 1)

            def pack_triangle(t):
                act.wait_ge(blocks_turned, t + 1)
                if t:
                    act.wait_ge(z_turned, t)
                for i, length, at in TRIANGLE[BY_VECTOR[t]:]:
                    last = act.copy(z[:, at:at + TRI * length].rearrange("p (r l) -> p r l", r=TRI),
                                    diagonal(i, length))
                last.then_inc(triangle_packed, 1)

            def copy_z(t, chunks=range(ZC)):
                first, count = chunks[0], len(chunks)
                act.wait_ge(z_turned, t + 1 + (first > 0))
                if t >= 2:
                    act.wait_ge(h1_done, 2 * (t - 1))
                act.copy(zt[:, t % 2, first:first + count, :],
                         z_bank(t, first)[:, first * P:(first + count) * P].rearrange("p (c b) -> p c b", c=count)) \
                   .then_inc(z_copied, 1)

            def relu1_low(t):
                act.wait_ge(h1_done, 2 * t + 1)
                if t == 0:
                    act.wait_ge(layers_landed, 64)
                if t >= 2:
                    act.wait_ge(h2_done, t - 1)
                for m in range(M1 // 2):
                    last = act.activation(h1[:, t % 2, m, :], ps_a[:, 0, m * P:(m + 1) * P], ACT.Relu, bias=b1_sb[:, m:m + 1])
                last.then_inc(h1_low_ready, 1)

            def relu2(t):
                if t >= 2:
                    act.wait_ge(y_done, t - 1)
                for m in range(M2):
                    act.wait_ge(h2_done, t + 1 + (m if t == TILES - 1 else 0))
                    act.activation(h2[:, t % 2, m, :], h2_block(t, m), ACT.Relu, bias=b2_sb[:, m:m + 1]) \
                       .then_inc(h2_ready, 1)

            def copy_y(t):
                act.wait_ge(y_done, t + 1)
                act.copy(y_sb[:, t * P:(t + 1) * P], ps_h2[0:1, 0, H2:H2 + P]).then_inc(y_copied, 1)

            act.wait_ge(row_id_landed, 16)
            act.mul(minus_row_id[:, :], row_id[:, CH - 1:CH], -1.0).then_inc(row_id_negated, 1)
            for h in range(WORK_RING):
                last_onehot(h)
                round_table(h)
            act.wait_ge(dense_landed, 16)
            act.copy(xt[:, :, 0], dense_sb[:, :]).then_inc(dense_copied, 1)
            for h in range(NOH):
                copy_lookup(h)
                if h + WORK_RING < NOH:
                    round_table(h + WORK_RING)
                    last_onehot(h + WORK_RING)
                for g in AFTER_LOOKUP[h]:
                    copy_group(g)
            copy_z(0)
            for t in range(TILES - 2):
                for g in AT_START[t]:
                    copy_group(g)
                relu1_low(t)
                for g in IN_MIDDLE[t]:
                    copy_group(g)
                relu2(t)
                for g in AT_END[t]:
                    copy_group(g)
                copy_z(t + 1)
                for g in AFTER_Z[t]:
                    copy_group(g)
                copy_y(t)
            t = TILES - 2
            relu1_low(t)
            for g in AT_START[t]:
                copy_group(g)
            pack_triangle(t + 1)
            copy_z(t + 1, range(1))
            relu2(t)
            copy_z(t + 1, range(1, ZC))
            copy_y(t)
            t = TILES - 1
            relu1_low(t)
            relu2(t)
            copy_y(t)


_INPUTS = ["ids"] + [f"tbl_{f}" for f in range(F)] + ["W_top1", "b_top1", "W_top2", "b_top2", "W_top3"]


def kernel(**inputs):
    import concourse.bacc as bacc
    from concourse.bass_utils import run_bass_kernel_spmd

    nc = bacc.Bacc("TRN2", target_bir_lowering=False, num_devices=1)
    arrays = {name: np.ascontiguousarray(inputs[name]) for name in _INPUTS}
    arrays["dense_by_column"] = np.ascontiguousarray(np.asarray(inputs["r_dense_features"]).T)
    arrays["ids_by_table"] = np.ascontiguousarray(np.asarray(inputs["ids"]).T)
    arrays["identity"] = np.eye(P, dtype=np.float32)
    arrays["table_rows"] = np.arange(P * CH, dtype=np.float32).reshape(P, CH)
    a = {name: nc.dram_tensor(name, x.shape, mybir.dt.from_np(x.dtype), kind="ExternalInput").ap()
         for name, x in arrays.items()}
    out = nc.dram_tensor("y", (B, 1), F32, kind="ExternalOutput").ap()
    build(nc, a["dense_by_column"], a["ids"], a["ids_by_table"], [a[f"tbl_{f}"] for f in range(F)],
          a["W_top1"], a["b_top1"], a["W_top2"], a["b_top2"], a["W_top3"], a["identity"], a["table_rows"], out)
    result = run_bass_kernel_spmd(nc, [arrays], core_ids=[0])
    return result.results[0]["y"]
```

```python
from contextlib import ExitStack

import numpy as np

import concourse.bass as bass
from concourse import mybir

ALU = mybir.AluOpType
ACT = mybir.ActivationFunctionType
F32 = mybir.dt.float32
F32R = mybir.dt.float32r
BF16 = mybir.dt.bfloat16
I32 = mybir.dt.int32

P = 128
B = 512
D = 128
F = 26
N = F + 1
NPAD = 32
TILES = B // P
BANK = 512
H1, H2 = 512, 256
M1, M2 = H1 // P, H2 // P

ONEHOT_TABLES = [4, 10, 11, 19, 20, 24, 25, 3, 8, 14]
LOOKUP_FROM = [0] * 8 + [P, 2 * P]
V = 1000
CH = 8
CH_V = CH - 1
VP = V // CH
VP_A = VP // 16 * 16
NOH = len(ONEHOT_TABLES)
WHOLE = LOOKUP_FROM.count(0)
TABLE_RING = 4
WORK_RING = 2
ROWS_RING = 3


def is_gathered(f, t):
    return f not in ONEHOT_TABLES or t * P < LOOKUP_FROM[ONEHOT_TABLES.index(f)]


GATHERED = [f for f in range(F) if is_gathered(f, 0)]
SOURCES = [[f + 1 for f in GATHERED if is_gathered(f, t)] for t in range(TILES)]
GROUPS = [(t, s[i:i + 4]) for t, s in enumerate(SOURCES) for i in range(0, len(s), 4)]
GROUPS[-1:] = [(TILES - 1, GROUPS[-1][1][:-1]), (TILES - 1, GROUPS[-1][1][-1:])]

AFTER_LOOKUP = [[], [0], [1], [2], [3], [4], [5], [6, 7], [8], [9, 10]]
IN_MIDDLE = [[11], [14], [16]]
AT_END = [[12, 13], [15], [17, 18]]
ORDER = sum(AFTER_LOOKUP, [])
for _t in range(TILES - 1):
    ORDER += IN_MIDDLE[_t] + AT_END[_t]
assert ORDER == list(range(len(GROUPS)))
GROUPS_UP_TO = [sum(t <= tile for t, _ in GROUPS) for tile in range(TILES)]

WARM_UP = 14
HIGH, LOW = PARTS = range(2)

TRI = 3
TRIANGLE = []
_at = 0
for _i in range(0, N, TRI):
    TRIANGLE.append((_i, N - 1 - _i, _at))
    _at += TRI * (N - 1 - _i)
ZC = -(-_at // P)
ZUSED = _at
FIRST_COPIES = sum(at < P for _, _, at in TRIANGLE)
FIRST_ROWS = FIRST_COPIES * TRI
BY_VECTOR = len(TRIANGLE) - 2


def runs(features):
    out = []
    for slot, n in enumerate(features):
        if out and out[-1][1] + out[-1][2] == n:
            out[-1][2] += 1
        else:
            out.append([slot, n, 1])
    return out


def weight_rows():
    first_row = [D + sum(N - 1 - a for a in range(i)) for i in range(N)]
    out = []
    for i, length, at in TRIANGLE:
        for u in range(TRI):
            row, z, left = first_row[i + u], at + u * length, N - 1 - (i + u)
            if out and out[-1][0] + out[-1][2] == row and out[-1][1] + out[-1][2] == z:
                out[-1][2] += left
            elif left > 0:
                out.append([row, z, left])
    cut = []
    for row, z, left in out:
        while left:
            k = min(left, P - z % P)
            cut.append((row, z, k))
            row, z, left = row + k, z + k, left - k
    return cut


def build(nc, dense_by_column, ids, ids_by_table, tables, w1, b1, w2, b2, w3, identity, table_rows, out):
    with ExitStack() as ctx:
        def sb(name, shape, dt):
            return ctx.enter_context(nc.sbuf_tensor(name, shape, dt))

        def sem(name):
            return ctx.enter_context(nc.semaphore(name))

        ident_sb = sb("ident_sb", [P, P], F32)
        row_id = sb("row_id", [P, CH], F32)
        minus_row_id = sb("minus_row_id", [P, 1], F32)
        distance = sb("distance", [VP, B], F32)
        ident = ident_sb[:, :]
        zeros = sb("zeros", [P, BANK], BF16)
        ids_sb = sb("ids_sb", [P, TILES, F], I32)
        dense_sb = sb("dense_sb", [D, B], F32)
        rows_sb = sb("rows_sb", [P, ROWS_RING, len(GATHERED), D], F32)
        xt = sb("xt", [P, B, N], F32)
        table_sb = sb("table_sb", [VP, TABLE_RING, CH * D], F32)
        parts_sb = [sb(f"part{i}_sb", [VP, WORK_RING, CH * D], F32R) for i in PARTS]
        idrow = sb("idrow", [P, TABLE_RING, B], I32)
        onehot = sb("onehot", [VP, WORK_RING, CH, B], F32R)
        zz = sb("zz", [P, N + 1, NPAD], F32)
        z = sb("z", [P, ZC * P], F32)
        zt = sb("zt", [P, 2, ZC, P], F32)
        h1 = sb("h1", [P, 2, M1, P], F32)
        h2 = sb("h2", [P, TILES, M2, P], F32)
        w1z = sb("w1z", [P, ZC, H1], F32)
        w1d = sb("w1d", [P, 3, H1], F32)
        w2_sb = sb("w2_sb", [P, M1, H2], F32)
        w3_sb = sb("w3_sb", [P, M2], F32)
        b1_sb = sb("b1_sb", [P, M1], F32)
        b2_sb = sb("b2_sb", [P, M2], F32)
        y_sb = sb("y_sb", [P, P], F32)

        def bank(name, banks=1):
            return ctx.enter_context(nc.psum_tensor(name, [P, banks, BANK], F32))

        ps_a = bank("ps_a", 2)
        ps_rows = bank("ps_rows", 2)
        ps_gram = bank("ps_gram", 2)
        ps_z = bank("ps_z")
        ps_h2 = bank("ps_h2")
        SPB = NPAD // 2

        ids_landed = sem("ids_landed")
        ident_landed = sem("ident_landed")
        row_id_landed = sem("row_id_landed")
        dense_landed = sem("dense_landed")
        w1d_landed = sem("w1d_landed")
        w1z_landed = sem("w1z_landed")
        layers_landed = sem("layers_landed")
        idrow_landed = [sem(f"idrow_landed{i}") for i in range(TABLE_RING)]
        table_landed = [sem(f"table_landed{i}") for i in range(TABLE_RING)]
        group_landed = [sem(f"group_landed{g}") for g in range(len(GROUPS))]
        zeros_ready = sem("zeros_ready")
        w1z_zeroed = sem("w1z_zeroed")
        gram_zeroed = sem("gram_zeroed")
        w1d_summed = sem("w1d_summed")
        onehot_ready = sem("onehot_ready")
        last_onehot_ready = sem("last_onehot_ready")
        dense_copied = sem("dense_copied")
        row_id_negated = sem("row_id_negated")
        distance_ready = sem("distance_ready")
        part_ready = [sem(f"part{i}_ready") for i in PARTS]
        lookup_done = sem("lookup_done")
        lookup_copied = sem("lookup_copied")
        group_turned = sem("group_turned")
        group_copied = sem("group_copied")
        gram_done = sem("gram_done")
        blocks_turned = sem("blocks_turned")
        first_chunk_packed = sem("first_chunk_packed")
        triangle_packed = sem("triangle_packed")
        z_turned = sem("z_turned")
        z_copied = sem("z_copied")
        h1_done = sem("h1_done")
        h1_low_ready = sem("h1_low_ready")
        h1_high_ready = sem("h1_high_ready")
        h2_done = sem("h2_done")
        h2_ready = sem("h2_ready")
        y_done = sem("y_done")
        y_copied = sem("y_copied")
        stored = sem("stored")

        def diagonal(i, length):
            flat, step = zz[:, :, :].rearrange("p m n -> p (m n)"), NPAD + 1
            first = i * step + 1
            return flat[:, first:first + TRI * step].rearrange("p (r l) -> p r l", r=TRI)[:, :, 0:length]

        def z_bank(t, c):
            return ps_rows[:, 0, :] if t == TILES - 1 and c == 0 else ps_z[:, 0, :]

        def h2_block(t, m):
            return ps_rows[:, 1, 0:P] if t == TILES - 1 and m == M2 - 1 else ps_h2[:, 0, m * P:(m + 1) * P]

        def y_row(t):
            return ps_h2[NPAD * t:NPAD * t + 1, 0, H2:H2 + P]

        W1Z = weight_rows()
        block = ctx.enter_context(nc.Block())

        @block.sync
        def _(sp):
            def load_table(h):
                s, f = h % TABLE_RING, ONEHOT_TABLES[h]
                if h >= TABLE_RING:
                    sp.wait_ge(lookup_done, h - TABLE_RING + 1)
                sp.dma_start(idrow[:, s, :], ids_by_table[f:f + 1, :].to_broadcast([P, B])).then_inc(idrow_landed[s], 16)
                rows = tables[f].rearrange("(p c) d -> p (c d)", c=CH)
                sp.dma_start(table_sb[0:VP_A, s, :], rows[0:VP_A, :]).then_inc(table_landed[s], 16)
                sp.dma_start(table_sb[VP_A:VP, s, :], rows[VP_A:VP, :]).then_inc(table_landed[s], 16)

            sp.dma_start(ids_sb[:, :, :], ids.rearrange("(t p) f -> p t f", p=P)).then_inc(ids_landed, 16)
            sp.dma_start(row_id[:, :], table_rows).then_inc(row_id_landed, 16)
            load_table(0)
            sp.dma_start(ident_sb[:, :], identity).then_inc(ident_landed, 16)
            sp.dma_start(dense_sb[:, :], dense_by_column).then_inc(dense_landed, 16)
            for h in range(1, TABLE_RING):
                load_table(h)
            sp.wait_ge(w1z_zeroed, 1)
            per_table = -(-len(W1Z) // (NOH - TABLE_RING))
            for h in range(TABLE_RING, NOH):
                load_table(h)
                if h == TABLE_RING:
                    sp.dma_start(w1d[:, 0, :], w1[0:D, :]).then_inc(w1d_landed, 16)
                    sp.dma_start(w1d[:, 1, :], w1[w1.shape[0] - D:, :]).then_inc(w1d_landed, 16)
                first = (h - TABLE_RING) * per_table
                for row, at, count in W1Z[first:first + per_table]:
                    sp.dma_start(w1z[at % P:at % P + count, at // P, :], w1[row:row + count, :]).then_inc(w1z_landed, 16)
            sp.dma_start(w2_sb[:, :, :], w2.rearrange("(m p) n -> p m n", p=P)).then_inc(layers_landed, 16)
            with nc.allow_non_contiguous_dma(reason="biases and the last layer's weights: a value per partition"):
                sp.dma_start(w3_sb[:, :], w3.rearrange("(m p) o -> p (m o)", p=P)).then_inc(layers_landed, 16)
                sp.dma_start(b1_sb[:, :], b1.rearrange("(m p) -> p m", p=P)).then_inc(layers_landed, 16)
                sp.dma_start(b2_sb[:, :], b2.rearrange("(m p) -> p m", p=P)).then_inc(layers_landed, 16)
            sp.wait_ge(y_copied, TILES)
            sp.dma_start(out.rearrange("(t p) o -> t (o p)", p=P), y_sb[0:P:NPAD, :]).then_inc(stored, 16)
            sp.wait_ge(stored, 16)

        @block.gpsimd
        def _(pool):
            pool.wait_ge(ids_landed, 16)
            for g, (t, features) in enumerate(GROUPS):
                if t >= ROWS_RING and t != GROUPS[g - 1][0]:
                    pool.wait_ge(group_turned, GROUPS_UP_TO[t - ROWS_RING])
                for n in features:
                    f = n - 1
                    pool.indirect_dma_start(
                        rows_sb[:, t % ROWS_RING, GATHERED.index(f), :], None, tables[f],
                        bass.IndirectOffsetOnAxis(ids_sb[:, t, f:f + 1], 0),
                    ).then_inc(group_landed[g], 16)

        @block.tensor
        def _(pe):
            def lookup(h):
                w, lo = h % WORK_RING, LOOKUP_FROM[h]
                if h >= 2:
                    pe.wait_ge(lookup_copied, h - 1)
                for part in PARTS:
                    pe.wait_ge(part_ready[part], h + 1)
                    for c in range(CH):
                        if part == HIGH and c < CH_V:
                            pe.wait_ge(onehot_ready, CH_V * h + c + 1)
                        elif part == HIGH:
                            pe.wait_ge(last_onehot_ready, h + 1)
                        last = pe.matmul(ps_a[:, h % 2, lo:], parts_sb[part][:, w, c * D:(c + 1) * D],
                                         onehot[:, w, c, lo:], start=(part == HIGH and c == 0),
                                         stop=(part == LOW and c == CH - 1))
                last.then_inc(lookup_done, 1)

            def turn_group(g):
                t, features = GROUPS[g]
                if g >= 2:
                    pe.wait_ge(group_copied, g - 1)
                if g == 0:
                    pe.wait_ge(ident_landed, 16)
                pe.wait_ge(group_landed[g], 16 * len(features))
                for slot, n in enumerate(features):
                    last = pe.transpose(ps_rows[:, g % 2, slot * P:(slot + 1) * P],
                                        rows_sb[:, t % ROWS_RING, GATHERED.index(n - 1), :], ident)
                last.then_inc(group_turned, 1)

            def gram(t, half):
                if half == 0:
                    pe.wait_ge(group_copied, GROUPS_UP_TO[t])
                    pe.wait_ge(lookup_copied, sum(lo < (t + 1) * P for lo in LOOKUP_FROM))
                    if t == 0:
                        pe.wait_ge(dense_copied, 1)
                        pe.wait_ge(gram_zeroed, 1)
                    else:
                        pe.wait_ge(blocks_turned, t)
                for s in range(SPB):
                    for j in range(P // NPAD):
                        x = xt[:, t * P + j * NPAD + half * SPB + s, :]
                        last = pe.matmul(ps_gram[j * NPAD:j * NPAD + N, half, s * N:(s + 1) * N], x, x,
                                         start=True, stop=True)
                if half == 1:
                    last.then_inc(gram_done, 1)

            def turn_z(t, chunks):
                if t < TILES - 1:
                    pe.wait_ge(triangle_packed, t + 1)
                elif 0 in chunks:
                    pe.wait_ge(first_chunk_packed, 1)
                else:
                    pe.wait_ge(triangle_packed, t + 2)
                if t:
                    pe.wait_ge(z_copied, t)
                for c in chunks:
                    last = pe.transpose(z_bank(t, c)[:, c * P:(c + 1) * P], z[:, c * P:(c + 1) * P], ident)
                last.then_inc(z_turned, 1)

            def layer1_dense(t):
                if t == 0:
                    pe.wait_ge(w1d_summed, 1)
                    pe.wait_ge(lookup_copied, NOH)
                else:
                    pe.wait_ge(h1_low_ready, t)
                    pe.wait_ge(h1_high_ready, t)
                for m in range(M1):
                    pe.matmul(ps_a[:, m // 2, (m % 2) * P:(m % 2 + 1) * P], w1d[:, 2, m * P:(m + 1) * P],
                              dense_sb[:, t * P:(t + 1) * P], start=(m % 2 == 0), stop=False, skip_group_check=True)

            def layer1_pairs(t, k, chunks=range(ZC)):
                if k == 0:
                    if t == 0:
                        pe.wait_ge(w1z_landed, 16 * len(W1Z))
                    pe.wait_ge(z_copied, t + 1 + (t == TILES - 1 and ZC - 1 in chunks))
                for m in range(2 * k, 2 * k + 2):
                    for c in chunks:
                        last = pe.matmul(ps_a[:, k, (m % 2) * P:(m % 2 + 1) * P], w1z[:, c, m * P:(m + 1) * P],
                                         zt[:, t % 2, c, :], start=False, stop=(c == ZC - 1), skip_group_check=True)
                if ZC - 1 in chunks:
                    last.then_inc(h1_done, 1)

            def layer2(t, half):
                if half == 0:
                    pe.wait_ge(layers_landed, 64)
                    if t:
                        pe.wait_ge(h2_ready, M2 * t)
                pe.wait_ge(h1_high_ready if half else h1_low_ready, t + 1)
                for k in range(half * M1 // 2, (half + 1) * M1 // 2):
                    for m in range(M2):
                        last = pe.matmul(ps_h2[:, 0, m * P:(m + 1) * P], w2_sb[:, k, m * P:(m + 1) * P], h1[:, t % 2, k, :],
                                         start=(k == 0 and m == 0), stop=(k == M1 - 1), skip_group_check=True)
                if half:
                    last.then_inc(h2_done, 1)

            def layer2_last():
                t = TILES - 1
                pe.wait_ge(y_copied, t)
                for half, ready in enumerate((h1_low_ready, h1_high_ready)):
                    pe.wait_ge(ready, t + 1)
                    for m in range(M2):
                        for k in range(half * M1 // 2, (half + 1) * M1 // 2):
                            last = pe.matmul(h2_block(t, m), w2_sb[:, k, m * P:(m + 1) * P], h1[:, t % 2, k, :],
                                             start=(k == 0), stop=(k == M1 - 1))
                        if half:
                            last.then_inc(h2_done, 1)

            def layer3(tiles):
                for k in range(M2):
                    if tiles[-1] == TILES - 1:
                        pe.wait_ge(h2_ready, M2 * (TILES - 1) + k + 1)
                    elif k == 0:
                        pe.wait_ge(h2_ready, M2 * (tiles[-1] + 1))
                    for t in tiles:
                        last = pe.matmul(y_row(t), w3_sb[:, k:k + 1], h2[:, t, k, :],
                                         start=(k == 0), stop=(k == M2 - 1))
                last.then_inc(y_done, 1)

            pe.wait_ge(zeros_ready, 1)
            for _ in range(WARM_UP):
                pe.matmul(ps_z[:, 0, :], zeros[:, 0:P], zeros[:, :], start=True, stop=True)

            for h in range(WHOLE):
                lookup(h)
                for g in AFTER_LOOKUP[h]:
                    turn_group(g)
            for half in range(2):
                gram(0, half)
            for h in range(WHOLE, NOH):
                lookup(h)
                for g in AFTER_LOOKUP[h]:
                    turn_group(g)
            turn_z(0, range(ZC))
            layer1_dense(0)
            for t in range(TILES - 2):
                gram(t + 1, 0)
                layer1_pairs(t, 0)
                for g in IN_MIDDLE[t]:
                    turn_group(g)
                layer1_pairs(t, 1)
                gram(t + 1, 1)
                layer2(t, 0)
                layer2(t, 1)
                for g in AT_END[t]:
                    turn_group(g)
                turn_z(t + 1, range(ZC))
                layer1_dense(t + 1)
            t = TILES - 2
            layer1_pairs(t, 0)
            for g in IN_MIDDLE[t]:
                turn_group(g)
            layer1_pairs(t, 1)
            for g in AT_END[t][:-1]:
                turn_group(g)
            layer2(t, 0)
            turn_group(AT_END[t][-1])
            layer2(t, 1)
            t = TILES - 1
            for half in range(2):
                gram(t, half)
            layer1_dense(t)
            turn_z(t, range(1))
            layer3(range(TILES - 1))
            layer1_pairs(t, 0, range(1))
            turn_z(t, range(1, ZC))
            layer1_pairs(t, 1, range(1))
            layer1_pairs(t, 0, range(1, ZC))
            layer1_pairs(t, 1, range(1, ZC))
            layer2_last()
            layer3([t])

        @block.vector
        def _(dve):
            dve.memset(zeros[:, :], 0.0).then_inc(zeros_ready, 1)
            dve.memset(w1z[:, :, :], 0.0).then_inc(w1z_zeroed, 1)
            dve.memset(ps_gram[:, :, 0:SPB * N], 0.0).then_inc(gram_zeroed, 1)
            dve.wait_ge(row_id_landed, 16)

            def prepare_lookup(h):
                s, w = h % TABLE_RING, h % WORK_RING
                dve.wait_ge(idrow_landed[s], 16 * (h // TABLE_RING + 1))
                if h >= WORK_RING:
                    dve.wait_ge(lookup_done, h - WORK_RING + 1)
                for c in range(CH_V):
                    dve.tensor_scalar(onehot[:, w, c, LOOKUP_FROM[h]:], idrow[0:VP, s, LOOKUP_FROM[h]:],
                                      row_id[0:VP, c:c + 1], None, ALU.is_equal).then_inc(onehot_ready, 1)
                dve.wait_ge(part_ready[HIGH], h + 1)
                dve.tensor_tensor(parts_sb[LOW][:, w, :], table_sb[:, s, :], parts_sb[HIGH][:, w, :].bitcast(F32),
                                  ALU.subtract).then_inc(part_ready[LOW], 1)

            for h in range(NOH):
                prepare_lookup(h)
            dve.memset(z[:, ZUSED:], 0.0)
            dve.wait_ge(w1d_landed, 32)
            dve.tensor_tensor(w1d[:, 2, :], w1d[:, 0, :], w1d[:, 1, :], ALU.add).then_inc(w1d_summed, 1)

            for t in range(TILES):
                dve.wait_ge(gram_done, t + 1)
                if t:
                    dve.wait_ge(triangle_packed, t)
                blocks = ps_gram[:, :, 0:SPB * N].rearrange("p k (s m) -> p m k s", m=N)
                if t < TILES - 1:
                    dve.transpose(zz[:, 0:N, :], blocks).then_inc(blocks_turned, 1)
                    dve.wait_ge(blocks_turned, t + 1)
                else:
                    dve.transpose(zz[:, 0:FIRST_ROWS, :], blocks[:, 0:FIRST_ROWS]).then_inc(blocks_turned, 1)
                    dve.transpose(zz[:, FIRST_ROWS:N, :], blocks[:, FIRST_ROWS:N]).then_inc(blocks_turned, 1)
                    dve.wait_ge(blocks_turned, t + 2)
                if t:
                    dve.wait_ge(z_turned, t)
                for i, length, at in TRIANGLE if t < TILES - 1 else TRIANGLE[FIRST_COPIES:BY_VECTOR]:
                    last = dve.tensor_copy(
                        z[:, at:at + TRI * length].rearrange("p (r l) -> p r l", r=TRI),
                        diagonal(i, length))
                last.then_inc(triangle_packed, 1)
                dve.wait_ge(h1_done, 2 * (t + 1))
                if t == 0:
                    dve.wait_ge(layers_landed, 64)
                if t >= 2:
                    dve.wait_ge(h2_done, t - 1)
                for m in range(M1 // 2, M1):
                    last = dve.tensor_scalar(h1[:, t % 2, m, :], ps_a[:, 1, (m % 2) * P:(m % 2 + 1) * P],
                                             b1_sb[:, m:m + 1], 0.0, ALU.add, ALU.max)
                last.then_inc(h1_high_ready, 1)

        @block.scalar
        def _(act):
            def round_table(h):
                s, w = h % TABLE_RING, h % WORK_RING
                act.wait_ge(table_landed[s], 32 * (h // TABLE_RING + 1))
                if h >= WORK_RING:
                    act.wait_ge(lookup_done, h - WORK_RING + 1)
                act.copy(parts_sb[HIGH][:, w, :], table_sb[:, s, :]).then_inc(part_ready[HIGH], 1)

            def last_onehot(h):
                s, w, lo = h % TABLE_RING, h % WORK_RING, LOOKUP_FROM[h]
                act.wait_ge(idrow_landed[s], 16 * (h // TABLE_RING + 1))
                if h == 0:
                    act.wait_ge(row_id_negated, 1)
                else:
                    act.wait_ge(last_onehot_ready, h)
                act.activation(distance[:, lo:], idrow[0:VP, s, lo:], ACT.Abs, bias=minus_row_id[0:VP, :]) \
                   .then_inc(distance_ready, 1)
                if h >= WORK_RING:
                    act.wait_ge(lookup_done, h - WORK_RING + 1)
                act.wait_ge(distance_ready, h + 1)
                act.activation(onehot[:, w, CH - 1, lo:], distance[:, lo:], ACT.Relu, bias=1.0, scale=-1.0) \
                   .then_inc(last_onehot_ready, 1)

            def copy_lookup(h):
                act.wait_ge(lookup_done, h + 1)
                lo = LOOKUP_FROM[h]
                act.copy(xt[:, lo:, ONEHOT_TABLES[h] + 1], ps_a[:, h % 2, lo:]).then_inc(lookup_copied, 1)

            def copy_group(g):
                t, features = GROUPS[g]
                act.wait_ge(group_turned, g + 1)
                for slot, n, count in runs(features):
                    last = act.copy(
                        xt[:, t * P:(t + 1) * P, n:n + count],
                        ps_rows[:, g % 2, slot * P:(slot + count) * P].rearrange("p (n b) -> p b n", n=count))
                last.then_inc(group_copied, 1)

            def pack_triangle(copies, turned, packed):
                act.wait_ge(blocks_turned, turned)
                act.wait_ge(z_turned, TILES - 1)
                for i, length, at in copies:
                    last = act.copy(z[:, at:at + TRI * length].rearrange("p (r l) -> p r l", r=TRI),
                                    diagonal(i, length))
                last.then_inc(packed, 1)

            def copy_z(t, chunks=range(ZC)):
                first, count = chunks[0], len(chunks)
                act.wait_ge(z_turned, t + 1 + (first > 0))
                if t >= 2:
                    act.wait_ge(h1_done, 2 * (t - 1))
                act.copy(zt[:, t % 2, first:first + count, :],
                         z_bank(t, first)[:, first * P:(first + count) * P].rearrange("p (c b) -> p c b", c=count)) \
                   .then_inc(z_copied, 1)

            def relu1_low(t):
                act.wait_ge(h1_done, 2 * t + 1)
                if t == 0:
                    act.wait_ge(layers_landed, 64)
                if t >= 2:
                    act.wait_ge(h2_done, t - 1)
                for m in range(M1 // 2):
                    last = act.activation(h1[:, t % 2, m, :], ps_a[:, 0, m * P:(m + 1) * P], ACT.Relu, bias=b1_sb[:, m:m + 1])
                last.then_inc(h1_low_ready, 1)

            def relu2(t):
                for m in range(M2):
                    act.wait_ge(h2_done, t + 1 + (m if t == TILES - 1 else 0))
                    act.activation(h2[:, t, m, :], h2_block(t, m), ACT.Relu, bias=b2_sb[:, m:m + 1]) \
                       .then_inc(h2_ready, 1)

            def copy_y(t):
                act.wait_ge(y_done, 2 if t == TILES - 1 else 1)
                act.copy(y_sb[NPAD * t:NPAD * t + 1, :], y_row(t)).then_inc(y_copied, 1)

            act.wait_ge(row_id_landed, 16)
            act.mul(minus_row_id[:, :], row_id[:, CH - 1:CH], -1.0).then_inc(row_id_negated, 1)
            for h in range(WORK_RING):
                last_onehot(h)
                round_table(h)
            act.wait_ge(dense_landed, 16)
            act.copy(xt[:, :, 0], dense_sb[:, :]).then_inc(dense_copied, 1)
            for h in range(NOH):
                copy_lookup(h)
                if h + WORK_RING < NOH:
                    round_table(h + WORK_RING)
                    last_onehot(h + WORK_RING)
                for g in AFTER_LOOKUP[h]:
                    copy_group(g)
            copy_z(0)
            for t in range(TILES - 2):
                relu1_low(t)
                for g in IN_MIDDLE[t]:
                    copy_group(g)
                relu2(t)
                for g in AT_END[t]:
                    copy_group(g)
                copy_z(t + 1)
            t = TILES - 2
            relu1_low(t)
            for g in IN_MIDDLE[t] + AT_END[t]:
                copy_group(g)
            relu2(t)
            pack_triangle(TRIANGLE[:FIRST_COPIES], TILES, first_chunk_packed)
            copy_z(t + 1, range(1))
            pack_triangle(TRIANGLE[BY_VECTOR:], TILES + 1, triangle_packed)
            copy_z(t + 1, range(1, ZC))
            for t in range(TILES - 1):
                copy_y(t)
            t = TILES - 1
            relu1_low(t)
            relu2(t)
            copy_y(t)


_INPUTS = ["ids"] + [f"tbl_{f}" for f in range(F)] + ["W_top1", "b_top1", "W_top2", "b_top2", "W_top3"]


def kernel(**inputs):
    import concourse.bacc as bacc
    from concourse.bass_utils import run_bass_kernel_spmd

    nc = bacc.Bacc("TRN2", target_bir_lowering=False, num_devices=1)
    arrays = {name: np.ascontiguousarray(inputs[name]) for name in _INPUTS}
    arrays["dense_by_column"] = np.ascontiguousarray(np.asarray(inputs["r_dense_features"]).T)
    arrays["ids_by_table"] = np.ascontiguousarray(np.asarray(inputs["ids"]).T)
    arrays["identity"] = np.eye(P, dtype=np.float32)
    arrays["table_rows"] = np.arange(P * CH, dtype=np.float32).reshape(P, CH)
    a = {name: nc.dram_tensor(name, x.shape, mybir.dt.from_np(x.dtype), kind="ExternalInput").ap()
         for name, x in arrays.items()}
    out = nc.dram_tensor("y", (B, 1), F32, kind="ExternalOutput").ap()
    build(nc, a["dense_by_column"], a["ids"], a["ids_by_table"], [a[f"tbl_{f}"] for f in range(F)],
          a["W_top1"], a["b_top1"], a["W_top2"], a["b_top2"], a["W_top3"], a["identity"], a["table_rows"], out)
    result = run_bass_kernel_spmd(nc, [arrays], core_ids=[0])
    return result.results[0]["y"]
```
